# Optimizing a Trainium2 kernel written in Bass

```python
import numpy as np
import jax
import jax.numpy as jnp

def _softmax(x, axis=-1):
    return jax.nn.softmax(x, axis=axis)

def _gelu(x):
    return jax.nn.gelu(x, approximate=True)

def _silu(x):
    return jax.nn.silu(x)

def _sigmoid(x):
    return jax.nn.sigmoid(x)

def _layernorm(x, axis=-1, eps=1e-05):
    m = jnp.mean(x, axis=axis, keepdims=True)
    v = jnp.var(x, axis=axis, keepdims=True)
    return (x - m) / jnp.sqrt(v + eps)

def _scatter_add(tgt, idx, src, axis=0):
    return tgt.at[idx].add(src)

def _segment_sum(src, seg, n):
    return jax.ops.segment_sum(src, seg, n)
kernel_name = 'mk_prb_d1_jaxref_r8_5cc6ad'

def setup_inputs(seed: int=0):
    np.random.seed(seed)
    _w = jnp.asarray

    def _L0_attn_setup():
        import jax, jax.numpy as jnp
        import numpy as np
        D = 128
        key = jax.random.key(seed)
        ks = jax.random.split(key, 7)
        s = 1.0 / np.sqrt(D)
        X = jax.random.normal(ks[0], (4, 256, D), dtype=jnp.float32)
        Wq = jax.random.uniform(ks[1], (D, D), jnp.float32, -s, s)
        Wk = jax.random.uniform(ks[2], (D, D), jnp.float32, -s, s)
        Wv = jax.random.uniform(ks[3], (D, D), jnp.float32, -s, s)
        bq = jax.random.uniform(ks[4], (D,), jnp.float32, -s, s)
        bk = jax.random.uniform(ks[5], (D,), jnp.float32, -s, s)
        bv = jax.random.uniform(ks[6], (D,), jnp.float32, -s, s)
        return {'X': X, 'Wq': Wq, 'bq': bq, 'Wk': Wk, 'bk': bk, 'Wv': Wv, 'bv': bv}
    _L0_attn_in = _L0_attn_setup()

    def _L0_ffn_setup():
        import jax, jax.numpy as jnp
        import numpy as np
        DIM = 128
        DEPTH = 6
        HEADS = 16
        DIM_HEAD = 64
        WINDOW = 32
        INNER = HEADS * DIM_HEAD
        DIM_INNER = int(DIM * 4 * 2 / 3)
        QK_SCALE = 8.0

        def shift_tokens(t):
            a, s = jnp.split(t, 2, -1)
            s = jnp.pad(s, ((0, 0), (1, 0), (0, 0)))[:, :-1]
            return jnp.concatenate([a, s], -1)

        def l2norm(t):
            return t / jnp.maximum(jnp.linalg.norm(t, axis=-1, keepdims=True), 1e-12)

        def rotate_half(x):
            x1, x2 = jnp.split(x, 2, -1)
            return jnp.concatenate([-x2, x1], -1)

        def rotary_tables(n):
            half = jnp.arange(0, DIM_HEAD, 2, dtype=jnp.float32)
            inv_freq = 1.0 / 10000.0 ** (half / DIM_HEAD)
            t = jnp.arange(n, dtype=jnp.float32)
            freqs = t[:, None] * inv_freq[None, :]
            freqs = jnp.concatenate([freqs, freqs], -1)
            base_scale = (half + 0.4 * DIM_HEAD) / (1.4 * DIM_HEAD)
            power = (t - n // 2) / (WINDOW // 2)
            scale = base_scale[None, :] ** power[:, None]
            scale = jnp.concatenate([scale, scale], -1)
            return (freqs, scale)

        def local_attention(q, k, v):
            b, h, n, d = q.shape
            w = WINDOW
            nw = n // w
            bq = q.reshape(b, h, nw, w, d)
            bk = k.reshape(b, h, nw, w, d)
            bv = v.reshape(b, h, nw, w, d)

            def look(t):
                p = jnp.pad(t, ((0, 0), (0, 0), (1, 0), (0, 0), (0, 0)))
                return jnp.concatenate([p[:, :, :nw], p[:, :, 1:]], axis=3)
            bk2, bv2 = (look(bk), look(bv))
            seq = jnp.arange(n).reshape(nw, w)
            seq_p = jnp.pad(seq, ((1, 0), (0, 0)), constant_values=-1)
            jt = jnp.concatenate([seq_p[:nw], seq_p[1:]], axis=1)
            it = seq[:, :, None]
            jb = jt[:, None, :]
            mask = (it < jb) | (it > jb + w) | (jb == -1)
            sim = jnp.einsum('bhwie,bhwje->bhwij', bq, bk2) * QK_SCALE
            sim = jnp.where(mask, -jnp.finfo(sim.dtype).max, sim)
            attn = jax.nn.softmax(sim, -1)
            out = jnp.einsum('bhwij,bhwje->bhwie', attn, bv2)
            return out.reshape(b, h, n, d)

        def attn_layer(x, Wqkv, qs, ksc, Wo):
            b, n, _ = x.shape
            qkv = x @ Wqkv
            q, k, v = jnp.split(qkv, 3, -1)
            sh = lambda t: t.reshape(b, n, HEADS, DIM_HEAD).transpose(0, 2, 1, 3)
            q, k, v = (sh(q), sh(k), sh(v))
            q = l2norm(q) * qs
            k = l2norm(k) * ksc
            freqs, scale = rotary_tables(n)
            cos, sin = (jnp.cos(freqs), jnp.sin(freqs))
            q = q * cos * scale + rotate_half(q) * sin * scale
            inv = 1.0 / scale
            k = k * cos * inv + rotate_half(k) * sin * inv
            out = local_attention(q, k, v)
            out = out.transpose(0, 2, 1, 3).reshape(b, n, INNER)
            return out @ Wo

        def ffn_layer(x, g, bln, W1, b1, W2, b2):
            mu = x.mean(-1, keepdims=True)
            var = ((x - mu) ** 2).mean(-1, keepdims=True)
            xn = (x - mu) / jnp.sqrt(var + 1e-05) * g + bln
            hg = xn @ W1 + b1
            a, gate = jnp.split(hg, 2, -1)
            return a * jax.nn.gelu(gate, approximate=False) @ W2 + b2
        key = jax.random.key(seed)
        ks = jax.random.split(key, 8)
        B, N = (2, 256)
        init = lambda k, shape: jax.random.normal(k, shape, jnp.float32) * 0.02
        return {'x': jax.random.normal(ks[0], (B, N, DIM), jnp.float32), 'Wqkv': init(ks[1], (DEPTH, DIM, 3 * INNER)), 'q_scale': jnp.ones((DEPTH, DIM_HEAD), jnp.float32), 'k_scale': jnp.ones((DEPTH, DIM_HEAD), jnp.float32), 'Wo': init(ks[2], (DEPTH, INNER, DIM)), 'ln_g': jnp.ones((DEPTH, DIM), jnp.float32), 'ln_b': jnp.zeros((DEPTH, DIM), jnp.float32), 'W1': init(ks[3], (DEPTH, DIM, 2 * DIM_INNER)), 'b1': jnp.zeros((DEPTH, 2 * DIM_INNER), jnp.float32), 'W2': init(ks[4], (DEPTH, DIM_INNER, DIM)), 'b2': jnp.zeros((DEPTH, DIM), jnp.float32)}
    _L0_ffn_in = _L0_ffn_setup()
    _d = {'L0_attn_X': _L0_attn_in['X'], 'L0_attn_Wq': _L0_attn_in['Wq'], 'L0_attn_bq': _L0_attn_in['bq'], 'L0_attn_Wk': _L0_attn_in['Wk'], 'L0_attn_bk': _L0_attn_in['bk'], 'L0_attn_Wv': _L0_attn_in['Wv'], 'L0_attn_bv': _L0_attn_in['bv'], 'L0_ffn_Wqkv': _L0_ffn_in['Wqkv'], 'L0_ffn_q_scale': _L0_ffn_in['q_scale'], 'L0_ffn_k_scale': _L0_ffn_in['k_scale'], 'L0_ffn_Wo': _L0_ffn_in['Wo'], 'L0_ffn_ln_g': _L0_ffn_in['ln_g'], 'L0_ffn_ln_b': _L0_ffn_in['ln_b'], 'L0_ffn_W1': _L0_ffn_in['W1'], 'L0_ffn_b1': _L0_ffn_in['b1'], 'L0_ffn_W2': _L0_ffn_in['W2'], 'L0_ffn_b2': _L0_ffn_in['b2']}
    _x0 = _d['L0_attn_X']
    _d['L0_attn_X'] = jax.random.normal(jax.random.fold_in(jax.random.key(seed), 1), (16, 256, 128), dtype=_x0.dtype)
    del _x0
    return _d

def reference(L0_attn_X, L0_attn_Wq, L0_attn_bq, L0_attn_Wk, L0_attn_bk, L0_attn_Wv, L0_attn_bv, L0_ffn_Wqkv, L0_ffn_q_scale, L0_ffn_k_scale, L0_ffn_Wo, L0_ffn_ln_g, L0_ffn_ln_b, L0_ffn_W1, L0_ffn_b1, L0_ffn_W2, L0_ffn_b2):

    def _L0_attn_ref(X, Wq, bq, Wk, bk, Wv, bv):
        import jax, jax.numpy as jnp
        import numpy as np
        D = 128
        N, S, Dm = X.shape
        scale = jnp.asarray(Dm ** 0.5, X.dtype)
        Q = jnp.einsum('nsd,ed->nse', X, Wq) + bq
        K = jnp.einsum('nsd,ed->nse', X, Wk) + bk
        V = jnp.einsum('nsd,ed->nse', X, Wv) + bv
        scores = jnp.einsum('nqd,nkd->nqk', Q, K) / scale
        causal = jnp.triu(jnp.ones((S, S), dtype=bool), k=1)
        scores = jnp.where(causal, -jnp.inf, scores)
        weights = jax.nn.softmax(scores, axis=-1)
        return jnp.einsum('nqk,nkd->nqd', weights, V)

    def _L0_ffn_ref(x, Wqkv, q_scale, k_scale, Wo, ln_g, ln_b, W1, b1, W2, b2):
        import jax, jax.numpy as jnp
        import numpy as np
        DIM = 128
        DEPTH = 6
        HEADS = 16
        DIM_HEAD = 64
        WINDOW = 32
        INNER = HEADS * DIM_HEAD
        DIM_INNER = int(DIM * 4 * 2 / 3)
        QK_SCALE = 8.0

        def shift_tokens(t):
            a, s = jnp.split(t, 2, -1)
            s = jnp.pad(s, ((0, 0), (1, 0), (0, 0)))[:, :-1]
            return jnp.concatenate([a, s], -1)

        def l2norm(t):
            return t / jnp.maximum(jnp.linalg.norm(t, axis=-1, keepdims=True), 1e-12)

        def rotate_half(x):
            x1, x2 = jnp.split(x, 2, -1)
            return jnp.concatenate([-x2, x1], -1)

        def rotary_tables(n):
            half = jnp.arange(0, DIM_HEAD, 2, dtype=jnp.float32)
            inv_freq = 1.0 / 10000.0 ** (half / DIM_HEAD)
            t = jnp.arange(n, dtype=jnp.float32)
            freqs = t[:, None] * inv_freq[None, :]
            freqs = jnp.concatenate([freqs, freqs], -1)
            base_scale = (half + 0.4 * DIM_HEAD) / (1.4 * DIM_HEAD)
            power = (t - n // 2) / (WINDOW // 2)
            scale = base_scale[None, :] ** power[:, None]
            scale = jnp.concatenate([scale, scale], -1)
            return (freqs, scale)

        def local_attention(q, k, v):
            b, h, n, d = q.shape
            w = WINDOW
            nw = n // w
            bq = q.reshape(b, h, nw, w, d)
            bk = k.reshape(b, h, nw, w, d)
            bv = v.reshape(b, h, nw, w, d)

            def look(t):
                p = jnp.pad(t, ((0, 0), (0, 0), (1, 0), (0, 0), (0, 0)))
                return jnp.concatenate([p[:, :, :nw], p[:, :, 1:]], axis=3)
            bk2, bv2 = (look(bk), look(bv))
            seq = jnp.arange(n).reshape(nw, w)
            seq_p = jnp.pad(seq, ((1, 0), (0, 0)), constant_values=-1)
            jt = jnp.concatenate([seq_p[:nw], seq_p[1:]], axis=1)
            it = seq[:, :, None]
            jb = jt[:, None, :]
            mask = (it < jb) | (it > jb + w) | (jb == -1)
            sim = jnp.einsum('bhwie,bhwje->bhwij', bq, bk2) * QK_SCALE
            sim = jnp.where(mask, -jnp.finfo(sim.dtype).max, sim)
            attn = jax.nn.softmax(sim, -1)
            out = jnp.einsum('bhwij,bhwje->bhwie', attn, bv2)
            return out.reshape(b, h, n, d)

        def attn_layer(x, Wqkv, qs, ksc, Wo):
            b, n, _ = x.shape
            qkv = x @ Wqkv
            q, k, v = jnp.split(qkv, 3, -1)
            sh = lambda t: t.reshape(b, n, HEADS, DIM_HEAD).transpose(0, 2, 1, 3)
            q, k, v = (sh(q), sh(k), sh(v))
            q = l2norm(q) * qs
            k = l2norm(k) * ksc
            freqs, scale = rotary_tables(n)
            cos, sin = (jnp.cos(freqs), jnp.sin(freqs))
            q = q * cos * scale + rotate_half(q) * sin * scale
            inv = 1.0 / scale
            k = k * cos * inv + rotate_half(k) * sin * inv
            out = local_attention(q, k, v)
            out = out.transpose(0, 2, 1, 3).reshape(b, n, INNER)
            return out @ Wo

        def ffn_layer(x, g, bln, W1, b1, W2, b2):
            mu = x.mean(-1, keepdims=True)
            var = ((x - mu) ** 2).mean(-1, keepdims=True)
            xn = (x - mu) / jnp.sqrt(var + 1e-05) * g + bln
            hg = xn @ W1 + b1
            a, gate = jnp.split(hg, 2, -1)
            return a * jax.nn.gelu(gate, approximate=False) @ W2 + b2
        for i in range(DEPTH):
            x = attn_layer(shift_tokens(x), Wqkv[i], q_scale[i], k_scale[i], Wo[i]) + x
            x = ffn_layer(shift_tokens(x), ln_g[i], ln_b[i], W1[i], b1[i], W2[i], b2[i]) + x
        return x
    x = L0_attn_X
    xn = _layernorm(x, axis=-1)
    x = x + _L0_attn_ref(xn, L0_attn_Wq, L0_attn_bq, L0_attn_Wk, L0_attn_bk, L0_attn_Wv, L0_attn_bv) + _L0_ffn_ref(xn, L0_ffn_Wqkv, L0_ffn_q_scale, L0_ffn_k_scale, L0_ffn_Wo, L0_ffn_ln_g, L0_ffn_ln_b, L0_ffn_W1, L0_ffn_b1, L0_ffn_W2, L0_ffn_b2)
    return x

_drawn_inputs = setup_inputs


def setup_inputs(seed=0):
    import zlib

    import numpy as np

    out = dict(_drawn_inputs(seed))
    spreads = {'L0_ffn_q_scale': (1.0, 0.6),
     'L0_ffn_k_scale': (1.0, 0.6),
     'L0_ffn_ln_g': (1.0, 0.6),
     'L0_ffn_ln_b': (0.0, 0.8),
     'L0_ffn_b1': (0.0, 0.8),
     'L0_ffn_b2': (0.0, 0.1)}
    factors = {'L0_attn_Wq': 3.678,
     'L0_attn_bq': 8.0,
     'L0_attn_Wk': 3.557,
     'L0_attn_bk': 64.0,
     'L0_ffn_W1': 3.643,
     'L0_ffn_W2': 3.578,
     'L0_attn_bv': 6.519}
    for name, (base, spread) in spreads.items():
        noise = np.random.default_rng([zlib.crc32(name.encode()), seed]).standard_normal(out[name].shape)
        drawn = base * np.exp(spread * noise) if base else spread * noise
        out[name] = jnp.asarray(drawn.astype(out[name].dtype))
    for name, factor in factors.items():
        out[name] = (out[name] * factor).astype(out[name].dtype)
    return out
```

```python
import concourse.bass as bass
from concourse import mybir
from contextlib import ExitStack

F32 = mybir.dt.float32
BF16 = mybir.dt.bfloat16
ALU = mybir.AluOpType
ACT = mybir.ActivationFunctionType
AX = mybir.AxisListType

P = 128
NB, NTOK, D = 16, 256, 128
DEPTH, HEADS, DH, WIN = 6, 16, 64, 32
INNER = HEADS * DH
FF = int(D * 4 * 2 / 3)
FC = -(-FF // 3)
FCHUNKS = [(c * FC, min(FC, FF - c * FC)) for c in range(3)]
TILES = NTOK // P
GPB = 4
GROUPS = NB * GPB
GW = 512
SCORE_SCALE = float(D) ** -0.5
LN_EPS = 1e-5
SUM_SCALE = 65536.0
LN_EXP_SET, GELU_SET = 6, 10


def live(part, u, lag):
    return {"first": u >= lag, "middle": True, "last": u < lag}[part]


def steps(eng, body):
    body("first", 0)
    with eng.Fori(1, NB) as b:
        body("middle", b)
    body("last", NB)


def load_tables(nc, number):
    nc.scalar.add_instruction(mybir.InstLoadActFuncSet(
        name=nc.get_next_instruction_name(), act_func_set_id=number, ins=[], outs=[]))


def heads(ap, n=8):
    return ap.rearrange("p (h d) -> p h d", h=n)


def each_head(ap, n):
    return ap.unsqueeze(2).to_broadcast([ap.shape[0], ap.shape[1], n])


def input_phase(nc, m, x, wqkv_dense, biases, bv):
    with ExitStack() as ctx:
        def sem(name):
            return ctx.enter_context(nc.semaphore(name))

        def sb(name, shape, dt=F32):
            return ctx.enter_context(nc.sbuf_tensor(name, shape, dt))

        banks = m["banks"]
        CH = 4
        CT = NB * TILES // CH
        w_raw = sb("dense_w_raw", [P, 3, D])
        w_t = sb("dense_w_t", [P, 3, D])
        bias_col = sb("dense_bias_col", [P, 2])
        bv_row = sb("dense_bv_row", [P, D])
        total = sb("ln_total", [P, NB * TILES])
        mean = sb("ln_mean", [P, NB * TILES])
        squares = sb("ln_squares", [P, CT * D])
        var = sb("ln_var", [P, NB * TILES])
        log_var = sb("ln_log", [P, NB * TILES])
        seed = sb("ln_seed", [P, NB * TILES])
        work = sb("ln_work", [P, NB * TILES])
        rstd = sb("ln_rstd", [P, NB * TILES])
        xn_tok = sb("xn_tok", [P, TILES, D])
        xn_ch = sb("xn_ch", [P, NTOK])
        qk = sb("dense_qk", [P, 2, NTOK])
        v = sb("dense_v", [P, TILES, D])
        rowmax = sb("dense_rowmax", [P, TILES])
        negmax = sb("dense_negmax", [P, TILES])
        prob = sb("dense_prob", [P, 3 * P])
        rowsum = sb("dense_rowsum", [P, TILES])
        rrow = sb("dense_rrow", [P, TILES])
        prob_t = sb("dense_prob_t", [P, 3 * P])
        xc = m["xn"].rearrange("p (n d) -> p n d", d=D)
        base = m["base"]

        x_in = [sem(f"x_in{c}") for c in range(CH)]
        w_in, b_in, mask_in, stage_in = sem("w_in"), sem("b_in"), sem("mask_in"), sem("stage_in")
        ident_zero, ident_ready, ones_ready = sem("ident_zero"), sem("ident_ready"), sem("ones_ready")
        state_zero, ident_bf, masks_bf = sem("state_zero"), sem("ident_bf"), sem("masks_bf")
        w_tr, w_ready = sem("w_tr"), sem("w_ready")
        total_ready, mean_ready, xc_ready = sem("total_ready"), sem("mean_ready"), sem("xc_ready")
        sq_ready, ss_ready, var_ready = sem("sq_ready"), sem("ss_ready"), sem("var_ready")
        log_ready, seed_ready, nw1, nw2 = sem("log_ready"), sem("seed_ready"), sem("nw1"), sem("nw2")
        rstd_ready = sem("rstd_ready")
        xn_ready, xnt_done, xnt_ready, state_copied = sem("xn_ready"), sem("xnt_done"), sem("xnt_ready"), sem("state_copied")
        qk_done, v_done, qk_ready, v_ready = sem("qk_done"), sem("v_done"), sem("qk_ready"), sem("v_ready")
        score_done, max_ready, neg_ready, prob_ready = sem("score_done"), sem("max_ready"), sem("neg_ready"), sem("prob_ready")
        pt_done, pt_ready, out_done, rrow_ready, base_ready = sem("pt_done"), sem("pt_ready"), sem("out_done"), sem("rrow_ready"), sem("base_ready")

        B_XT, B_QK, B_V, B_S, B_PT, B_O = banks[0], banks[1], banks[2], banks[3], banks[4], banks[5]

        def passes(eng, body):
            body("first", 0)
            with eng.Fori(1, NB) as b:
                body("middle", b)
            body("last", NB)

        with nc.Block() as block:

            @block.sync
            def _(sp):
                sp.dma_start(w_raw[:, :, :], wqkv_dense.rearrange("w e d -> e w d")).then_inc(w_in, 16)
                xv = x.rearrange("b (t p) d -> p (b t) d", p=P)
                for c in range(CH):
                    sp.dma_start(base[:, c * CT:(c + 1) * CT, :], xv[:, c * CT:(c + 1) * CT, :]).then_inc(x_in[c], 16)
                sp.dma_start(bias_col[:, :], biases.rearrange("w e -> e w")).then_inc(b_in, 16)
                sp.dma_start(bv_row[:, :], bv.rearrange("(a e) -> a e", a=1).to_broadcast([P, D])).then_inc(b_in, 16)
                sp.dma_start(m["mask_stage"][:, :], m["masks_dram"]).then_inc(mask_in, 16)
                sp.dma_start(m["rotary"][:, :, :, :], m["rotary_dram"]).then_inc(stage_in, 16)
                sp.wait_ge(stage_in, 16)

            @block.gpsimd
            def _(pool):
                nc.gpsimd.memset(m["ident"][:, :], 0.0).then_inc(ident_zero, 1)
                pool.wait_ge(ident_zero, 1)
                nc.gpsimd.affine_select(out=m["ident"][:, :], in_=m["ident"][:, :], compare_op=ALU.not_equal,
                                        fill=1.0, base=0, pattern=[[-1, P]], channel_multiplier=1).then_inc(ident_ready, 1)
                nc.gpsimd.memset(m["mean_w"][:, :], 1.0 / D).then_inc(ones_ready, 1)
                nc.gpsimd.memset(m["eps"][:, :], LN_EPS)
                for h in range(2):
                    nc.gpsimd.memset(m["k_t"][h][:, :, 0:WIN], 0.0).then_inc(state_zero, 1)
                    nc.gpsimd.memset(m["v_late"][h][0:WIN, :], 0.0).then_inc(state_zero, 1)
                pool.wait_ge(state_zero, 4)
                nc.gpsimd.memset(m["state"][D // 2:, :, 0:1], 0.0).then_inc(state_zero, 1)
                pool.wait_ge(state_zero, 5)

                def state_from_xn(b):
                    pool.wait_ge(xnt_ready, b + 1)
                    nc.gpsimd.tensor_copy(m["state"][0:64, bass.ds(b, 1), 0:NTOK], xn_ch[0:64, :].unsqueeze(1))
                    nc.gpsimd.tensor_copy(m["state"][64:P, bass.ds(b, 1), 1:NTOK + 1],
                                          xn_ch[64:P, :].unsqueeze(1)).then_inc(state_copied, 1)

                with pool.Fori(0, NB) as b:
                    state_from_xn(b)
                pool.wait_ge(state_copied, NB)

            @block.scalar
            def _(act):
                load_tables(nc, LN_EXP_SET)
                act.wait_ge(w_tr, 1)
                nc.scalar.activation(w_t[:, :, :], B_V[:, 0:3 * D].rearrange("p (w e) -> p w e", w=3), ACT.Copy).then_inc(w_ready, 1)
                act.wait_ge(ident_ready, 1)
                nc.scalar.activation(m["ident_bf"][:, :], m["ident"][:, :], ACT.Copy).then_inc(ident_bf, 1)
                act.wait_ge(mask_in, 16)
                nc.scalar.activation(m["masks"][:, :], m["mask_stage"][:, :], ACT.Copy).then_inc(masks_bf, 1)
                for c in range(CH):
                    act.wait_ge(xc_ready, c + 1)
                    if c:
                        act.wait_ge(ss_ready, c)
                    nc.scalar.activation(squares[:, :].rearrange("p (n d) -> p n d", d=D), xc[:, c * CT:(c + 1) * CT, :],
                                         ACT.Square).then_inc(sq_ready, 1)
                act.wait_ge(var_ready, 1)
                nc.scalar.activation(log_var[:, :], var[:, :], ACT.Ln).then_inc(log_ready, 1)
                act.wait_ge(log_ready, 1)
                nc.scalar.activation(seed[:, :], log_var[:, :], ACT.Exp, scale=-0.5).then_inc(seed_ready, 1)
                act.wait_ge(b_in, 32)

                def body(part, b):
                    if part != "last":
                        act.wait_ge(xnt_done, b + 1)
                        if part != "first":
                            act.wait_ge(state_copied, b)
                            act.wait_ge(v_done, b)
                        nc.scalar.activation(xn_ch[:, :], B_XT[:, 0:NTOK], ACT.Copy).then_inc(xnt_ready, 1)
                    if part != "first":
                        act.wait_ge(neg_ready, b)
                        nc.scalar.activation(prob[:, 0:P], B_S[:, 0:P], ACT.Exp, bias=negmax[:, 0:1],
                                             scale=SCORE_SCALE, accum_out=rowsum[:, 0:1])
                        nc.scalar.activation(prob[:, P:3 * P], B_S[:, P:3 * P], ACT.Exp, bias=negmax[:, 1:2],
                                             scale=SCORE_SCALE, accum_out=rowsum[:, 1:2]).then_inc(prob_ready, 1)
                    if part != "last":
                        act.wait_ge(qk_done, b + 1)
                        if part != "first":
                            act.wait_ge(score_done, b)
                        nc.scalar.activation(qk[:, 0, :], B_QK[:, 0:NTOK], ACT.Identity, bias=bias_col[:, 0:1])
                        nc.scalar.activation(qk[:, 1, :], B_QK[:, NTOK:2 * NTOK], ACT.Identity,
                                             bias=bias_col[:, 1:2]).then_inc(qk_ready, 1)
                    if part != "first":
                        act.wait_ge(pt_done, b)
                        nc.scalar.activation(prob_t[:, :], B_PT[:, 0:3 * P], ACT.Copy).then_inc(pt_ready, 1)

                passes(act, body)

            @block.tensor
            def _(pe):
                pe.wait_ge(w_in, 16)
                pe.wait_ge(ident_ready, 1)
                for w in range(3):
                    last = nc.tensor.transpose(B_V[:, w * D:(w + 1) * D], w_raw[:, w, :], m["ident"][:, :])
                last.then_inc(w_tr, 1)
                pe.wait_ge(w_ready, 1)
                pe.wait_ge(ident_bf, 1)
                pe.wait_ge(masks_bf, 1)

                def body(part, b):
                    if part != "last":
                        pe.wait_ge(xn_ready, b + 1)
                        if part != "first":
                            pe.wait_ge(xnt_ready, b)
                        for t in range(TILES):
                            last = nc.tensor.transpose(B_XT[:, t * P:(t + 1) * P], xn_tok[:, t, :], m["ident"][:, :])
                        last.then_inc(xnt_done, 1)
                    if part != "first":
                        pe.wait_ge(qk_ready, b)
                        nc.tensor.matmul(B_S[:, 0:3 * P], m["ident_bf"][:, :], m["masks"][:, 2 * P:5 * P],
                                         start=True, stop=False, skip_group_check=True)
                        nc.tensor.matmul(B_S[:, 0:P], qk[:, 0, 0:P], qk[:, 1, 0:P], start=False, stop=True, skip_group_check=True)
                        nc.tensor.matmul(B_S[:, P:3 * P], qk[:, 0, P:2 * P], qk[:, 1, :], start=False, stop=True,
                                         skip_group_check=True).then_inc(score_done, 1)
                    if part != "last":
                        pe.wait_ge(xnt_ready, b + 1)
                        if part != "first":
                            pe.wait_ge(qk_ready, b)
                        nc.tensor.matmul(B_QK[:, 0:NTOK], w_t[:, 0, :], xn_ch[:, :], start=True, stop=True)
                        nc.tensor.matmul(B_QK[:, NTOK:2 * NTOK], w_t[:, 1, :], xn_ch[:, :], start=True, stop=True).then_inc(qk_done, 1)
                        if part != "first":
                            pe.wait_ge(v_ready, b)
                        for t in range(TILES):
                            last = nc.tensor.matmul(B_V[:, t * D:(t + 1) * D], xn_ch[:, t * P:(t + 1) * P], w_t[:, 2, :],
                                                    start=True, stop=True)
                        last.then_inc(v_done, 1)
                    if part != "first":
                        pe.wait_ge(prob_ready, b)
                        for c in range(3):
                            last = nc.tensor.transpose(B_PT[:, c * P:(c + 1) * P], prob[:, c * P:(c + 1) * P], m["ident"][:, :])
                        last.then_inc(pt_done, 1)
                        pe.wait_ge(pt_ready, b)
                        if part == "last":
                            pe.wait_ge(base_ready, NB - 1)
                        nc.tensor.matmul(B_O[:, 0:D], prob_t[:, 0:P], v[:, 0, :], start=True, stop=True)
                        nc.tensor.matmul(B_O[:, D:2 * D], prob_t[:, P:2 * P], v[:, 0, :], start=True, stop=False)
                        nc.tensor.matmul(B_O[:, D:2 * D], prob_t[:, 2 * P:3 * P], v[:, 1, :], start=False, stop=True).then_inc(out_done, 1)

                passes(pe, body)

            @block.vector
            def _(dve):
                for c in range(CH):
                    part = slice(c * CT, (c + 1) * CT)
                    dve.wait_ge(x_in[c], 16)
                    nc.vector.tensor_reduce(total[:, part], base[:, part, :], AX.X, ALU.add).then_inc(total_ready, 1)
                    dve.wait_ge(total_ready, c + 1)
                    nc.vector.tensor_scalar(mean[:, part], total[:, part], 1.0 / D, None, ALU.mult).then_inc(mean_ready, 1)
                    dve.wait_ge(mean_ready, c + 1)
                    nc.vector.tensor_tensor(xc[:, part, :], base[:, part, :], each_head(mean[:, part], D),
                                            ALU.subtract).then_inc(xc_ready, 1)
                    dve.wait_ge(sq_ready, c + 1)
                    nc.vector.tensor_reduce(total[:, part], squares[:, :].rearrange("p (n d) -> p n d", d=D),
                                            AX.X, ALU.add).then_inc(ss_ready, 1)
                dve.wait_ge(ss_ready, CH)
                nc.vector.tensor_scalar(var[:, :], total[:, :], 1.0 / D, LN_EPS, ALU.mult, ALU.add).then_inc(var_ready, 1)
                dve.wait_ge(seed_ready, 1)
                nc.vector.tensor_tensor(work[:, :], seed[:, :], seed[:, :], ALU.mult).then_inc(nw1, 1)
                dve.wait_ge(nw1, 1)
                nc.vector.scalar_tensor_tensor(out=work[:, :], in0=work[:, :], scalar=-0.5, in1=var[:, :],
                                               op0=ALU.mult, op1=ALU.mult).then_inc(nw2, 1)
                dve.wait_ge(nw2, 1)
                nc.vector.scalar_tensor_tensor(out=rstd[:, :], in0=work[:, :], scalar=1.5, in1=seed[:, :],
                                               op0=ALU.add, op1=ALU.mult).then_inc(rstd_ready, 1)
                dve.wait_ge(rstd_ready, 1)
                dve.wait_ge(b_in, 32)

                def body(part, b):
                    if part != "last":
                        if part != "first":
                            dve.wait_ge(xnt_done, b)
                        nc.vector.tensor_tensor(xn_tok[:, :, :], xc[:, bass.ds(b * TILES, TILES), :],
                                                each_head(rstd[:, bass.ds(b * TILES, TILES)], D), ALU.mult).then_inc(xn_ready, 1)
                    if part != "first":
                        dve.wait_ge(score_done, b)
                        nc.vector.tensor_reduce(rowmax[:, 0:1], B_S[:, 0:P], AX.X, ALU.max)
                        nc.vector.tensor_reduce(rowmax[:, 1:2], B_S[:, P:3 * P], AX.X, ALU.max).then_inc(max_ready, 1)
                        dve.wait_ge(max_ready, b)
                        nc.vector.tensor_scalar(negmax[:, :], rowmax[:, :], -SCORE_SCALE, None, ALU.mult).then_inc(neg_ready, 1)
                        dve.wait_ge(out_done, b)
                        nc.vector.reciprocal(rrow[:, :], rowsum[:, :]).then_inc(rrow_ready, 1)
                        dve.wait_ge(rrow_ready, b)
                        for t in range(TILES):
                            last = nc.vector.scalar_tensor_tensor(
                                out=base[:, bass.ds((b - 1) * TILES + t, 1), :], in0=B_O[:, t * D:(t + 1) * D].unsqueeze(1),
                                scalar=rrow[:, t:t + 1], in1=base[:, bass.ds((b - 1) * TILES + t, 1), :], op0=ALU.mult, op1=ALU.add)
                        last.then_inc(base_ready, 1)
                    if part != "last":
                        dve.wait_ge(v_done, b + 1)
                        nc.vector.tensor_tensor(v[:, :, :], B_V[:, 0:NTOK].rearrange("p (t d) -> p t d", t=TILES),
                                                bv_row[:, :].unsqueeze(1).to_broadcast([P, TILES, D]), ALU.add).then_inc(v_ready, 1)

                passes(dve, body)
                dve.wait_ge(base_ready, NB)


def layer_phase(nc, m, wqkv, q_scale, k_scale, wo, ln_g, ln_b, w1, b1, w2, b2):
    with ExitStack() as ctx:
        def sem(name):
            return ctx.enter_context(nc.semaphore(name))

        def sb(name, shape, dt=F32):
            return ctx.enter_context(nc.sbuf_tensor(name, shape, dt))

        banks = m["banks"]
        state, xn, ident, ident_bf, masks = m["state"], m["xn"], m["ident"], m["ident_bf"], m["masks"]
        k_t, v_late = m["k_t"], m["v_late"]

        wqkv_sb = sb("wqkv_sb", [P, 3 * INNER])
        wo_sb = sb("wo_sb", [P, INNER // P, D])
        w1_sb = sb("w1_sb", [P, 2 * FF])
        w2_sb = sb("w2_sb", [P, 3, D])
        b1_sb = sb("b1_sb", [P, 2, 3])
        cols = sb("cols", [P, 3])
        scales = sb("scales", [P, 2, DH])
        rot = sb("rot", [P, 4, TILES, DH])
        xs = sb("xs", [P, TILES, P])
        sq = [sb("sq_q", [P, GW]), sb("sq_k", [P, GW])]
        by_cos = [sb("cos_q", [P, GW]), sb("cos_k", [P, GW])]
        by_sin = [sb("sin_q", [P, GW]), sb("sin_k", [P, GW])]
        unit = [sb("unit_q", [P, GW]), sb("unit_k", [P, GW])]
        sums = sb("sums", [P, 16])
        clamped = sb("clamped", [P, 16])
        logs = sb("logs", [P, 16])
        seeds = sb("seeds", [P, 16])
        newton = sb("newton", [P, 16])
        rnorm = sb("rnorm", [P, 16])
        q_t = sb("q_t", [P, 4, P])
        v_tok = [sb(f"v_tok{i}", [P, GW]) for i in range(GPB)]
        rowmax = sb("rowmax", [P, 8])
        shifted = sb("shifted", [P, GW])
        prob = sb("prob", [P, GW])
        half_sum = sb("half_sum", [P, 8, DH // 2])
        rowsum = sb("rowsum", [P, 8])
        rrow = sb("rrow", [P, 8])
        prob_t = sb("prob_t", [P, GW])
        o_tok = sb("o_tok", [P, GW])
        o_t = sb("o_t", [P, GW])
        centred = sb("centred", [P, NTOK])
        centred_sq = sb("centred_sq", [P, NTOK])
        log_var = sb("log_var", [P, NTOK])
        rstd = sb("rstd", [P, NTOK])
        normed = sb("normed", [P, NTOK])
        gate = sb("gate", [P, 3, 512])
        inner = sb("inner", [P, 3, 512])

        B_Q, B_K, B_V, B_QT, B_KT, B_S, B_P, B_Y = banks

        attn_w_in, ffn_w_in, tables = sem("attn_w_in"), sem("ffn_w_in"), sem("tables")
        xs_ready = sem("xs_ready")
        q_done, k_done, v_done = sem("q_done"), sem("k_done"), sem("v_done")
        sq_ready = [sem("sqq_ready"), sem("sqk_ready")]
        rotated = [sem("rotated_q"), sem("rotated_k")]
        added = [sem("added_q"), sem("added_k")]
        unit_ready = [sem("unit_q_ready"), sem("unit_k_ready")]
        sums_ready, clamped_ready, logs_ready, seeds_ready = sem("sums_ready"), sem("clamped_ready"), sem("logs_ready"), sem("seeds_ready")
        newton1, newton2, rnorm_ready = sem("newton1"), sem("newton2"), sem("rnorm_ready")
        qt_done, kt_done, qt_ready, kt_ready = sem("qt_done"), sem("kt_done"), sem("qt_ready"), sem("kt_ready")
        v_ready = sem("v_ready")
        late_ready = [sem(f"late_ready{u}") for u in range(GPB)]
        LATE = [16, 16, 32, 32]
        score_done, max_ready, shifted_ready, exp_ready = sem("score_done"), sem("max_ready"), sem("shifted_ready"), sem("exp_ready")
        half_ready, rowsum_ready, rrow_ready, prob_ready = sem("half_ready"), sem("rowsum_ready"), sem("rrow_ready"), sem("prob_ready")
        pt_done, pt_ready, pv_done, o_ready = sem("pt_done"), sem("pt_ready"), sem("pv_done"), sem("o_ready")
        ot_done, ot_ready, wo_done = sem("ot_done"), sem("ot_ready"), sem("wo_done")
        attn_added = sem("attn_added")
        mean_done, centred_ready, csq_ready, var_done = sem("mean_done"), sem("centred_ready"), sem("csq_ready"), sem("var_done")
        logv_ready, rstd_ready, normed_ready, xn_ready = sem("logv_ready"), sem("rstd_ready"), sem("normed_ready"), sem("xn_ready")
        gate_done, value_done, gate_ready, inner_ready = sem("gate_done"), sem("value_done"), sem("gate_ready"), sem("inner_ready")
        ffn_done, ffn_added = sem("ffn_done"), sem("ffn_added")

        BLOCKS = NB // 2
        ATTN_LOADS, FFN_LOADS = 4, 10

        with nc.Block() as block:

            @block.sync
            def _(sp):
                def load_attention(l):
                    one = bass.ds(l, 1)
                    sp.dma_start(wqkv_sb[:, :], wqkv[one, :, :].rearrange("l c n -> (l c) n")).then_inc(attn_w_in, 16)
                    sp.dma_start(wo_sb[:, :, :], wo[one, :, :].rearrange("l (k p) n -> p (l k) n", p=P)).then_inc(attn_w_in, 16)
                    for i, s in enumerate((q_scale, k_scale)):
                        sp.dma_start(scales[:, i, :], s[one, :].to_broadcast([P, DH])).then_inc(attn_w_in, 16)

                def load_ffn(l):
                    one = bass.ds(l, 1)
                    sp.dma_start(w1_sb[:, :], w1[one, :, :].rearrange("l c n -> (l c) n")).then_inc(ffn_w_in, 16)
                    sp.dma_start(w2_sb[0:FC, 0:2, :], w2[one, 0:2 * FC, :].rearrange("l (c p) n -> p (l c) n", p=FC)).then_inc(ffn_w_in, 16)
                    sp.dma_start(w2_sb[0:FF - 2 * FC, 2, :], w2[one, 2 * FC:FF, :].rearrange("l p n -> (l p) n")).then_inc(ffn_w_in, 16)
                    for i in range(2):
                        sp.dma_start(b1_sb[0:FC, i, 0:2], b1[one, i * FF:i * FF + 2 * FC].rearrange("l (c p) -> p (l c)", p=FC)).then_inc(ffn_w_in, 16)
                        sp.dma_start(b1_sb[0:FF - 2 * FC, i, 2:3], b1[one, i * FF + 2 * FC:(i + 1) * FF].rearrange("l p -> p l")).then_inc(ffn_w_in, 16)
                    for i, c in enumerate((ln_g, ln_b, b2)):
                        sp.dma_start(cols[:, i:i + 1], c[one, :].rearrange("l p -> p l")).then_inc(ffn_w_in, 16)

                def layer(l):
                    g0 = l * GROUPS
                    def body(b):
                        for u in range(GPB):
                            sp.wait_ge(v_ready, g0 + b * GPB + u + 1)
                            sp.dma_start(v_late[u][WIN:P, :], v_tok[u][0:P - WIN, :]).then_inc(late_ready[u], 16)
                            if u >= 2:
                                sp.dma_start(v_late[u][0:WIN, :], v_tok[u - 2][P - WIN:P, :]).then_inc(late_ready[u], 16)

                    with sp.Fori(0, NB) as b:
                        body(b)

                load_attention(0)
                load_ffn(0)
                with sp.Fori(0, DEPTH - 1) as l:
                    layer(l)
                    sp.wait_ge(xn_ready, (l + 1) * NB)
                    load_attention(l + 1)
                    sp.wait_ge(ffn_added, (l + 1) * BLOCKS)
                    load_ffn(l + 1)
                layer(DEPTH - 1)
                sp.wait_ge(ffn_added, DEPTH * BLOCKS)

            @block.gpsimd
            def _(pool):
                with pool.Fori(0, DEPTH) as l:
                    g0 = l * GROUPS
                    pool.wait_ge(attn_w_in, (l + 1) * ATTN_LOADS * 16)
                    halves = lambda ap: ap.rearrange("p t (a d) -> p t a d", a=2)
                    for i in range(2):
                        scale = scales[:, i, :].unsqueeze(1).to_broadcast([P, TILES, DH])
                        nc.gpsimd.tensor_tensor(rot[:, 2 * i, :, :], m["rotary"][:, 2 * i, :, :], scale, ALU.mult)
                        last = nc.gpsimd.tensor_tensor(halves(rot[:, 2 * i + 1, :, :]), halves(m["rotary"][:, 2 * i + 1, :, :]),
                                                       halves(scale)[:, :, ::-1, :], ALU.mult)
                    last.then_inc(tables, 1)

                    def body(part, b):
                        base = pool.snap(g0 + b * GPB)
                        for u in range(GPB):
                            if live(part, u, 2):
                                n = base + (u - 2)
                                p3 = prob[:, :].rearrange("p (h j) -> p h j", h=8)
                                pool.wait_ge(exp_ready, n + 1)
                                nc.gpsimd.tensor_tensor(half_sum[:, :, :], p3[:, :, 0:DH // 2], p3[:, :, DH // 2:DH],
                                                        ALU.add).then_inc(half_ready, 1)
                                pool.wait_ge(rrow_ready, n + 1)
                                nc.gpsimd.tensor_tensor(p3, p3, each_head(rrow[:, :], DH), ALU.mult).then_inc(prob_ready, 1)
                            if part != "last":
                                n = base + u
                                for i in range(2):
                                    pool.wait_ge(rotated[i], n + 1)
                                    nc.gpsimd.tensor_tensor(by_cos[i][:, :], by_cos[i][:, :], by_sin[i][:, :],
                                                            ALU.add).then_inc(added[i], 1)

                    steps(pool, body)

            @block.scalar
            def _(act):
                with act.Fori(0, DEPTH) as l:
                    g0, b0 = act.snap(l * GROUPS), act.snap(l * NB)
                    load_tables(nc, LN_EXP_SET)
                    act.wait_ge(ffn_w_in, (l + 1) * FFN_LOADS * 16)

                    def body(part, b):
                        base = act.snap(g0 + b * GPB)
                        for u in range(GPB):
                            if part != "last" and u % 2 == 0:
                                t = u // 2
                                if part != "first":
                                    act.wait_ge(v_done, base + (u - 2))
                                nc.scalar.activation(xs[:, t, :].unsqueeze(1), state[:, bass.ds(b, 1), t * P:(t + 1) * P],
                                                     ACT.Copy).then_inc(xs_ready, 1)
                            if live(part, u, 1):
                                n, h, t = base + (u - 1), (u - 1) % 2, (u - 1) % 4 // 2
                                act.wait_ge(qt_done, n + 1)
                                if not (part == "first" and u == 1):
                                    act.wait_ge(score_done, n)
                                nc.scalar.activation(q_t[:, :, :], B_QT[:, :].rearrange("p (a t) -> p a t", a=4),
                                                     ACT.Copy).then_inc(qt_ready, 1)
                                act.wait_ge(kt_done, n + 1)
                                nc.scalar.activation(k_t[h][:, :, WIN + t * P:WIN + (t + 1) * P],
                                                     B_KT[:, :].rearrange("p (a t) -> p a t", a=4), ACT.Copy).then_inc(kt_ready, 1)
                            if live(part, u, 3):
                                n = base + (u - 3)
                                act.wait_ge(ot_done, n + 1)
                                if not (part == "first" and u == 3):
                                    act.wait_ge(wo_done, n)
                                nc.scalar.activation(o_t[:, :], B_V[:, :], ACT.Copy).then_inc(ot_ready, 1)
                            if part != "last":
                                n = base + u
                                for i, done in enumerate((q_done, k_done)):
                                    act.wait_ge(done, n + 1)
                                    if not (part == "first" and u == 0):
                                        act.wait_ge(sums_ready, n)
                                    nc.scalar.activation(sq[i][:, :], (B_Q, B_K)[i][:, :], ACT.Square).then_inc(sq_ready[i], 1)
                                act.wait_ge(v_done, n + 1)
                                if part != "first":
                                    act.wait_ge(pv_done, n + 1 - GPB)
                                    if u < 2:
                                        act.wait_ge(late_ready[u + 2], (b0 + b) * LATE[u + 2])
                                nc.scalar.activation(v_tok[u][:, :], B_V[:, :], ACT.Copy).then_inc(v_ready, 1)
                            if part != "first" and u == 3:
                                act.wait_ge(centred_ready, b0 + b)
                                nc.scalar.activation(centred_sq[:, :], centred[:, :], ACT.Square).then_inc(csq_ready, 1)
                            if live(part, u, 2):
                                n = base + (u - 2)
                                act.wait_ge(pt_done, n + 1)
                                if not (part == "first" and u == 2):
                                    act.wait_ge(pv_done, n)
                                nc.scalar.activation(prob_t[:, :], B_P[:, :], ACT.Copy).then_inc(pt_ready, 1)
                            if part != "first" and u == 3:
                                k = b0 + b
                                act.wait_ge(var_done, k)
                                nc.scalar.activation(log_var[:, :], B_S[:, 0:NTOK], ACT.Ln, bias=m["eps"][:, 0:1]).then_inc(logv_ready, 1)
                                act.wait_ge(logv_ready, k)
                                nc.scalar.activation(rstd[:, :], log_var[:, :], ACT.Exp, scale=-0.5).then_inc(rstd_ready, 1)
                            if part != "last":
                                n = base + u
                                act.wait_ge(clamped_ready, n + 1)
                                nc.scalar.activation(logs[:, :], clamped[:, :], ACT.Ln).then_inc(logs_ready, 1)
                                act.wait_ge(logs_ready, n + 1)
                                nc.scalar.activation(seeds[:, :], logs[:, :], ACT.Exp, scale=-0.5).then_inc(seeds_ready, 1)
                            if live(part, u, 1):
                                n = base + (u - 1)
                                act.wait_ge(shifted_ready, n + 1)
                                if not (part == "first" and u == 1):
                                    act.wait_ge(pt_done, n)
                                nc.scalar.activation(prob[:, :], shifted[:, :], ACT.Exp).then_inc(exp_ready, 1)
                            if live(part, u, 2):
                                n = base + (u - 2)
                                act.wait_ge(pv_done, n + 1)
                                if not (part == "first" and u == 2):
                                    act.wait_ge(ot_done, n)
                                nc.scalar.activation(o_tok[:, :], B_P[:, :], ACT.Copy).then_inc(o_ready, 1)
                            if part != "first" and u == 3:
                                act.wait_ge(normed_ready, b0 + b)
                                nc.scalar.activation(xn[:, bass.ds((b - 1) * NTOK, NTOK)], normed[:, :], ACT.Identity,
                                                     bias=cols[:, 1:2]).then_inc(xn_ready, 1)

                    steps(act, body)

                    load_tables(nc, GELU_SET)
                    with act.Fori(0, BLOCKS) as j:
                        k0 = act.snap((l * BLOCKS + j) * 3)
                        for c, (_, w) in enumerate(FCHUNKS):
                            k = k0 + c
                            act.wait_ge(gate_done, k + 1)
                            nc.scalar.activation(gate[0:w, c, :], banks[2 * c][0:w, :], ACT.Gelu,
                                                 bias=b1_sb[0:w, 1, c:c + 1]).then_inc(gate_ready, 1)
                    act.wait_ge(ffn_added, (l + 1) * BLOCKS)

            @block.tensor
            def _(pe):
                def scores(n, h, t):
                    nc.tensor.matmul(B_S[:, :], ident_bf[:, :],
                                     masks[:, t * P:(t + 1) * P].unsqueeze(1).to_broadcast([P, 4, P]),
                                     start=True, stop=False, skip_group_check=True)
                    for hp in range(4):
                        for wp in range(2):
                            for wi in range(2):
                                for par in range(2):
                                    w, r = 2 * wp + wi, 64 * par
                                    o = 32 * (2 * par + wi)
                                    last = nc.tensor.matmul(
                                        B_S[o:o + WIN, hp * P + wp * 64:hp * P + wp * 64 + 64],
                                        q_t[r:r + 64, hp, w * WIN:(w + 1) * WIN],
                                        k_t[h][r:r + 64, hp, t * P + w * WIN:t * P + w * WIN + 2 * WIN],
                                        start=False, stop=True, skip_group_check=True)
                    last.then_inc(score_done, 1)

                def values(i):
                    for hp in range(4):
                        for par in range(2):
                            for wi in range(2):
                                for wp in range(2):
                                    w, r = 2 * wp + wi, 64 * wp
                                    v = v_tok[i] if wi else v_late[i]
                                    col = (2 * hp + par) * DH
                                    last = nc.tensor.matmul(
                                        B_P[w * WIN:(w + 1) * WIN, col:col + DH],
                                        prob_t[r:r + 64, hp * P + par * 64 + wi * WIN:hp * P + par * 64 + (wi + 1) * WIN],
                                        v[r:r + 64, col:col + DH], start=True, stop=True, skip_group_check=True)
                    last.then_inc(pv_done, 1)

                with pe.Fori(0, DEPTH) as l:
                    g0, b0 = pe.snap(l * GROUPS), pe.snap(l * NB)
                    pe.wait_ge(attn_w_in, (l + 1) * ATTN_LOADS * 16)

                    def body(part, b):
                        base = pe.snap(g0 + b * GPB)
                        for u in range(GPB):
                            if live(part, u, 1):
                                n = base + (u - 1)
                                for i, bank in enumerate((B_QT, B_KT)):
                                    pe.wait_ge(unit_ready[i], n + 1)
                                    if not (part == "first" and u == 1):
                                        pe.wait_ge((qt_ready, kt_ready)[i], n)
                                    for c in range(4):
                                        last = nc.tensor.transpose(bank[:, c * P:(c + 1) * P], unit[i][:, c * P:(c + 1) * P], ident[:, :])
                                    last.then_inc((qt_done, kt_done)[i], 1)
                            if live(part, u, 3):
                                n = base + (u - 3)
                                pe.wait_ge(o_ready, n + 1)
                                if part != "last":
                                    pe.wait_ge(v_ready, n + 3)
                                else:
                                    pe.wait_ge(v_ready, g0 + GROUPS)
                                for c in range(4):
                                    last = nc.tensor.transpose(B_V[:, c * P:(c + 1) * P], o_tok[:, c * P:(c + 1) * P], ident[:, :])
                                last.then_inc(ot_done, 1)
                            if part != "first" and u == 3:
                                pe.wait_ge(attn_added, b0 + b)
                                if part == "last":
                                    pe.wait_ge(o_ready, g0 + GROUPS)
                                nc.tensor.matmul(B_P[:, 0:NTOK], m["mean_w"][:, :], state[:, bass.ds(b - 1, 1), 0:NTOK],
                                                 start=True, stop=True).then_inc(mean_done, 1)
                            if part != "last":
                                n, h, t = base + u, u % 2, u // 2
                                if u % 2 == 0:
                                    pe.wait_ge(xs_ready, (b0 + b) * 2 + t + 1)
                                for i, (bank, done) in enumerate(((B_Q, q_done), (B_K, k_done))):
                                    if not (part == "first" and u == 0):
                                        pe.wait_ge(rotated[i], n)
                                    nc.tensor.matmul(bank[:, :], xs[:, t, :], wqkv_sb[:, i * INNER + h * GW:i * INNER + (h + 1) * GW],
                                                     start=True, stop=True).then_inc(done, 1)
                                if part == "middle" or u == 3:
                                    pe.wait_ge(ot_ready, n - 2)
                                elif not (part == "first" and u == 0):
                                    pe.wait_ge(v_ready, n)
                                nc.tensor.matmul(B_V[:, :], xs[:, t, :], wqkv_sb[:, 2 * INNER + h * GW:2 * INNER + (h + 1) * GW],
                                                 start=True, stop=True).then_inc(v_done, 1)
                            if live(part, u, 2):
                                i = (u - 2) % 4
                                n = base + (u - 2)
                                pe.wait_ge(prob_ready, n + 1)
                                pe.wait_ge(late_ready[i], (b0 + b + (1 if u >= 2 else 0)) * LATE[i])
                                if not (part == "first" and u == 2):
                                    pe.wait_ge(o_ready, n)
                                if part == "middle" and u == 3:
                                    pe.wait_ge(centred_ready, b0 + b)
                                for c in range(4):
                                    last = nc.tensor.transpose(B_P[:, c * P:(c + 1) * P], prob[:, c * P:(c + 1) * P], ident[:, :])
                                last.then_inc(pt_done, 1)
                            if live(part, u, 3):
                                i = (u - 3) % 4
                                n, h, t = base + (u - 3), i % 2, i // 2
                                pe.wait_ge(ot_ready, n + 1)
                                if part == "last" and u == 1:
                                    pe.wait_ge(pt_ready, n + 2)
                                if i == 0 and part != "first":
                                    pe.wait_ge(attn_added, b0 + b)
                                for c in range(4):
                                    last = nc.tensor.matmul(B_Y[:, t * P:(t + 1) * P], wo_sb[:, 4 * h + c, :], o_t[:, c * P:(c + 1) * P],
                                                            start=(i == 0 and c == 0), stop=True, skip_group_check=True)
                                last.then_inc(wo_done, 1)
                            if part != "first" and u == 3:
                                pe.wait_ge(csq_ready, b0 + b)
                                if part == "middle":
                                    pe.wait_ge(shifted_ready, base + (u - 1))
                                nc.tensor.matmul(B_S[:, 0:NTOK], m["mean_w"][:, :], centred_sq[:, :],
                                                 start=True, stop=True).then_inc(var_done, 1)
                            if live(part, u, 1):
                                i = (u - 1) % 4
                                n = base + (u - 1)
                                pe.wait_ge(qt_ready, n + 1)
                                pe.wait_ge(kt_ready, n + 1)
                                if live(part, u, 2):
                                    pe.wait_ge(pt_ready, n)
                                if not (part == "first" and u == 1):
                                    pe.wait_ge(shifted_ready, n)
                                if part == "middle" and u == 3:
                                    pe.wait_ge(logv_ready, b0 + b)
                                scores(n, i % 2, i // 2)
                            if live(part, u, 2):
                                i = (u - 2) % 4
                                values(i)

                    steps(pe, body)

                    pe.wait_ge(ffn_w_in, (l + 1) * FFN_LOADS * 16)
                    pe.wait_ge(xn_ready, b0 + NB)
                    j0 = pe.snap(l * BLOCKS)

                    def up(c, j, first):
                        lo, w = FCHUNKS[c]
                        if not first:
                            pe.wait_ge(inner_ready, (j0 + j - 1) * 3 + c + 1)
                        rhs = xn[:, bass.ds(j * 512, 512)]
                        nc.tensor.matmul(banks[2 * c][0:w, :], w1_sb[:, FF + lo:FF + lo + w], rhs, start=True, stop=True).then_inc(gate_done, 1)
                        nc.tensor.matmul(banks[2 * c + 1][0:w, :], w1_sb[:, lo:lo + w], rhs, start=True, stop=True).then_inc(value_done, 1)

                    def down(c, j, first=False):
                        w = FCHUNKS[c][1]
                        pe.wait_ge(inner_ready, (j0 + j) * 3 + c + 1)
                        if c == 0 and not first:
                            pe.wait_ge(ffn_added, j0 + j)
                        last = nc.tensor.matmul(banks[6][:, :], w2_sb[0:w, c, :], inner[0:w, c, :], start=(c == 0), stop=(c == 2))
                        if c == 2:
                            last.then_inc(ffn_done, 1)

                    def block_body(j, first):
                        up(0, j, first)
                        if not first:
                            down(2, j - 1)
                        up(1, j, first)
                        down(0, j, first)
                        up(2, j, first)
                        down(1, j)

                    block_body(0, True)
                    with pe.Fori(1, BLOCKS) as j:
                        block_body(j, False)
                    down(2, BLOCKS - 1)

            @block.vector
            def _(dve):
                with dve.Fori(0, DEPTH) as l:
                    g0, b0 = dve.snap(l * GROUPS), dve.snap(l * NB)
                    dve.wait_ge(tables, l + 1)

                    def body(part, b):
                        base = dve.snap(g0 + b * GPB)
                        for u in range(GPB):
                            def rotate(i):
                                n, t = base + u, u // 2
                                src = (B_Q, B_K)[i]
                                dve.wait_ge(sq_ready[i], n + 1)
                                nc.vector.tensor_tensor(heads(by_cos[i][:, :]), heads(src[:, :]),
                                                        rot[:, 2 * i, t, :].unsqueeze(1).to_broadcast([P, 8, DH]), ALU.mult)
                                four = lambda ap: ap.rearrange("p (h a d) -> p h a d", h=8, a=2)
                                nc.vector.tensor_tensor(
                                    four(by_sin[i][:, :]), four(src[:, :])[:, :, ::-1, :],
                                    rot[:, 2 * i + 1, t, :].rearrange("p (a d) -> p a d", a=2).unsqueeze(1).to_broadcast([P, 8, 2, DH // 2]),
                                    ALU.mult).then_inc(rotated[i], 1)

                            if part != "last":
                                rotate(0)
                            if live(part, u, 2):
                                n = base + (u - 2)
                                dve.wait_ge(half_ready, n + 1)
                                nc.vector.tensor_reduce(rowsum[:, :], half_sum[:, :, :], AX.X, ALU.add).then_inc(rowsum_ready, 1)
                                dve.wait_ge(rowsum_ready, n + 1)
                                nc.vector.reciprocal(rrow[:, :], rowsum[:, :]).then_inc(rrow_ready, 1)
                            if part != "last":
                                rotate(1)
                            if part != "first" and u == 3:
                                k = b0 + b
                                dve.wait_ge(mean_done, k)
                                nc.vector.tensor_tensor(centred[:, :].unsqueeze(1), state[:, bass.ds(b - 1, 1), 0:NTOK],
                                                        B_P[:, 0:NTOK].unsqueeze(1), ALU.subtract).then_inc(centred_ready, 1)
                            if part != "last":
                                n = base + u
                                for i in range(2):
                                    last = nc.vector.tensor_reduce(sums[:, 8 * i:8 * i + 8], heads(sq[i][:, :]), AX.X, ALU.add)
                                last.then_inc(sums_ready, 1)
                                dve.wait_ge(sums_ready, n + 1)
                                nc.vector.tensor_scalar(clamped[:, :], sums[:, :], 1e-24, SUM_SCALE, ALU.max, ALU.mult).then_inc(clamped_ready, 1)
                                dve.wait_ge(seeds_ready, n + 1)
                                nc.vector.tensor_tensor(newton[:, :], seeds[:, :], seeds[:, :], ALU.mult).then_inc(newton1, 1)
                                dve.wait_ge(newton1, n + 1)
                                nc.vector.scalar_tensor_tensor(out=newton[:, :], in0=newton[:, :], scalar=-0.5 * SUM_SCALE ** 0.5,
                                                               in1=clamped[:, :], op0=ALU.mult, op1=ALU.mult).then_inc(newton2, 1)
                                dve.wait_ge(newton2, n + 1)
                                nc.vector.scalar_tensor_tensor(out=rnorm[:, :], in0=newton[:, :], scalar=1.5 * SUM_SCALE ** 0.5,
                                                               in1=seeds[:, :], op0=ALU.add, op1=ALU.mult).then_inc(rnorm_ready, 1)
                                dve.wait_ge(rnorm_ready, n + 1)
                                for i in range(2):
                                    dve.wait_ge(added[i], n + 1)
                                    if not (part == "first" and u == 0):
                                        dve.wait_ge((qt_done, kt_done)[i], n)
                                    nc.vector.tensor_tensor(heads(unit[i][:, :]), heads(by_cos[i][:, :]),
                                                            each_head(rnorm[:, 8 * i:8 * i + 8], DH), ALU.mult).then_inc(unit_ready[i], 1)
                            if part != "first" and u == 2:
                                dve.wait_ge(wo_done, base)
                                one = bass.ds(b - 1, 1)
                                for lo, late in ((0, 0), (64, 1)):
                                    at = state[lo:lo + 64, one, late:late + NTOK]
                                    last = nc.vector.tensor_tensor(at, at, B_Y[lo:lo + 64, 0:NTOK].unsqueeze(1), ALU.add)
                                last.then_inc(attn_added, 1)
                            if part != "first" and u == 3:
                                k = b0 + b
                                dve.wait_ge(rstd_ready, k)
                                nc.vector.scalar_tensor_tensor(out=normed[:, :], in0=centred[:, :], scalar=cols[:, 0:1], in1=rstd[:, :],
                                                               op0=ALU.mult, op1=ALU.mult).then_inc(normed_ready, 1)
                            if live(part, u, 1):
                                n = base + (u - 1)
                                dve.wait_ge(score_done, n + 1)
                                nc.vector.tensor_reduce(rowmax[:, :], heads(B_S[:, :]), AX.X, ALU.max).then_inc(max_ready, 1)
                                dve.wait_ge(max_ready, n + 1)
                                if not (part == "first" and u == 1):
                                    dve.wait_ge(exp_ready, n)
                                nc.vector.tensor_tensor(heads(shifted[:, :]), heads(B_S[:, :]), each_head(rowmax[:, :], DH),
                                                        ALU.subtract).then_inc(shifted_ready, 1)

                    steps(dve, body)

                    j0 = dve.snap(l * BLOCKS)

                    def glu(c, j):
                        w = FCHUNKS[c][1]
                        k = (j0 + j) * 3 + c
                        dve.wait_ge(value_done, k + 1)
                        dve.wait_ge(gate_ready, k + 1)
                        nc.vector.scalar_tensor_tensor(out=inner[0:w, c, :], in0=banks[2 * c + 1][0:w, :], scalar=b1_sb[0:w, 0, c:c + 1],
                                                       in1=gate[0:w, c, :], op0=ALU.add, op1=ALU.mult).then_inc(inner_ready, 1)

                    def add_block(j):
                        dve.wait_ge(ffn_done, j0 + j + 1)
                        for lo, late in ((0, 0), (64, 1)):
                            at = state[lo:lo + 64, bass.ds(j * 2, 2), late:late + NTOK]
                            last = nc.vector.scalar_tensor_tensor(
                                out=at, in0=banks[6][lo:lo + 64, :].rearrange("p (b t) -> p b t", b=2), scalar=cols[lo:lo + 64, 2:3],
                                in1=at, op0=ALU.add, op1=ALU.add)
                        last.then_inc(ffn_added, 1)

                    for c in range(3):
                        glu(c, 0)
                    with dve.Fori(1, BLOCKS) as j:
                        glu(0, j)
                        add_block(j - 1)
                        glu(1, j)
                        glu(2, j)
                    add_block(BLOCKS - 1)


def output_phase(nc, m, out):
    with ExitStack() as ctx:
        def sem(name):
            return ctx.enter_context(nc.semaphore(name))

        banks, state, base, ident = m["banks"], m["state"], m["base"], m["ident"]
        final = [ctx.enter_context(nc.sbuf_tensor(f"final{t}", [P, P], F32)) for t in range(TILES)]
        out_tok = [ctx.enter_context(nc.sbuf_tensor(f"out_tok{t}", [P, P], F32)) for t in range(TILES)]
        copied, transposed, summed = ([sem(f"{name}{t}") for t in range(TILES)] for name in ("copied", "transposed", "summed"))
        stored = [sem(f"stored{t}") for t in range(TILES)]

        with nc.Block() as block:

            def passes(eng, body):
                body(0, True)
                with eng.Fori(1, NB) as b:
                    body(b, False)

            @block.scalar
            def _(act):
                def body(b, first):
                    for t in range(TILES):
                        if not first:
                            act.wait_ge(transposed[t], b)
                        for lo, late in ((0, 0), (64, 1)):
                            last = nc.scalar.activation(final[t][lo:lo + 64, :].unsqueeze(1),
                                                        state[lo:lo + 64, bass.ds(b, 1), t * P + late:(t + 1) * P + late], ACT.Copy)
                        last.then_inc(copied[t], 1)

                passes(act, body)

            @block.tensor
            def _(pe):
                def body(b, first):
                    for t in range(TILES):
                        pe.wait_ge(copied[t], b + 1)
                        if not first:
                            pe.wait_ge(summed[t], b)
                        nc.tensor.transpose(banks[t][:, 0:P], final[t][:, :], ident[:, :]).then_inc(transposed[t], 1)

                passes(pe, body)

            @block.vector
            def _(dve):
                def body(b, first):
                    for t in range(TILES):
                        dve.wait_ge(transposed[t], b + 1)
                        if not first:
                            dve.wait_ge(stored[t], b * 16)
                        nc.vector.tensor_tensor(out_tok[t][:, :].unsqueeze(1), base[:, bass.ds(b * TILES + t, 1), :],
                                                banks[t][:, 0:P].unsqueeze(1), ALU.add).then_inc(summed[t], 1)

                passes(dve, body)

            @block.sync
            def _(sp):
                with sp.Fori(0, NB) as b:
                    for t in range(TILES):
                        sp.wait_ge(summed[t], b + 1)
                        sp.dma_start(out[bass.ds(b, 1), t * P:(t + 1) * P, :].rearrange("b p d -> (b p) d"),
                                     out_tok[t][:, :]).then_inc(stored[t], 16)
                for t in range(TILES):
                    sp.wait_ge(stored[t], NB * 16)


def block_kernel(nc, t):
    with ExitStack() as ctx:
        ctx.enter_context(nc.allow_non_contiguous_dma(reason="bias and scale vectors as columns"))

        def sb(name, shape, dt=F32):
            return ctx.enter_context(nc.sbuf_tensor(name, shape, dt))

        m = {
            "banks": [ctx.enter_context(nc.psum_tensor(f"bank{i}", [P, GW], F32)) for i in range(8)],
            "state": sb("state", [P, NB, NTOK + 1]),
            "xn": sb("xn", [P, NB * NTOK]),
            "base": sb("base", [P, NB * TILES, D]),
            "ident": sb("ident", [P, P]),
            "ident_bf": sb("ident_bf_sb", [P, P], BF16),
            "mean_w": sb("mean_w", [P, P]),
            "eps": sb("eps", [P, 1]),
            "masks": sb("masks_sb", [P, 5 * P], BF16),
            "mask_stage": sb("mask_stage", [P, 5 * P]),
            "rotary": sb("rotary_sb", [P, 4, TILES, DH]),
            "k_t": [sb(f"k_t{h}", [P, 4, WIN + NTOK]) for h in range(2)],
            "v_late": [sb(f"v_late{u}", [P, GW]) for u in range(GPB)],
            "masks_dram": t["masks"], "rotary_dram": t["rotary"],
        }
        input_phase(nc, m, t["x"], t["w_dense"], t["b_dense"], t["bv"])
        layer_phase(nc, m, *(t[k] for k in ("wqkv", "q_scale", "k_scale", "wo", "ln_g", "ln_b", "w1", "b1", "w2", "b2")))
        output_phase(nc, m, t["out"])


def shape_constants():
    import numpy as np
    f = np.float32
    half = np.arange(0, DH, 2, dtype=f)
    inv_freq = (f(1.0) / f(10000.0) ** (half / f(DH))).astype(f)
    pos = np.arange(NTOK, dtype=f)
    freqs = pos[:, None] * inv_freq[None, :]
    base_scale = (half + f(0.4 * DH)) / f(1.4 * DH)
    power = (pos - NTOK // 2) / f(WIN // 2)
    scale = (base_scale[None, :] ** power[:, None]).astype(f)
    cos, sin = np.cos(freqs).astype(f), np.sin(freqs).astype(f)
    two = lambda a, b: np.concatenate([a, b], -1)
    tables = np.stack([two(cos * scale, cos * scale) * f(8.0), two(-sin * scale, sin * scale) * f(8.0),
                       two(cos / scale, cos / scale), two(-sin / scale, sin / scale)])
    rotary = tables.reshape(4, TILES, P, DH).transpose(2, 0, 1, 3).astype(f)

    off = f(-3.0e38)
    masks = np.zeros((P, 5, P), f)
    i = np.arange(P)[:, None] % WIN
    wi = np.arange(P)[:, None] // WIN % 2
    wp, jj = np.arange(P)[None, :] // 64, np.arange(P)[None, :] % 64
    for t in range(TILES):
        allowed = (jj - WIN <= i) & (i <= jj)
        if t == 0:
            allowed &= ~((2 * wp + wi == 0) & (jj < WIN))
        masks[:, t, :] = np.where(allowed, f(0), off)
    causal = np.where(np.arange(P)[None, :] <= np.arange(P)[:, None], f(0), off)
    masks[:, 2, :] = causal
    masks[:, 4, :] = causal
    return np.ascontiguousarray(rotary), masks.reshape(P, 5 * P)


def kernel(**inputs):
    import numpy as np
    import concourse.bacc as bacc
    from concourse.bass_utils import run_bass_kernel_spmd

    a = {k: np.asarray(v) for k, v in inputs.items()}
    rotary, masks = shape_constants()
    arrays = {
        "x": a["L0_attn_X"],
        "w_dense": np.stack([a["L0_attn_Wq"], a["L0_attn_Wk"], a["L0_attn_Wv"]]),
        "b_dense": np.stack([a["L0_attn_bq"], a["L0_attn_bk"]]),
        "bv": a["L0_attn_bv"],
        "wqkv": a["L0_ffn_Wqkv"], "q_scale": a["L0_ffn_q_scale"], "k_scale": a["L0_ffn_k_scale"], "wo": a["L0_ffn_Wo"],
        "ln_g": a["L0_ffn_ln_g"], "ln_b": a["L0_ffn_ln_b"], "w1": a["L0_ffn_W1"], "b1": a["L0_ffn_b1"],
        "w2": a["L0_ffn_W2"], "b2": a["L0_ffn_b2"],
        "rotary": rotary, "masks": masks,
    }
    nc = bacc.Bacc("TRN2", target_bir_lowering=False, num_devices=1)
    feed, t = {}, {}
    for name, array in arrays.items():
        feed[f"{name}_dram"] = np.ascontiguousarray(array)
        t[name] = nc.dram_tensor(f"{name}_dram", array.shape, F32, kind="ExternalInput").ap()
    t["out"] = nc.dram_tensor("out_dram", (NB, NTOK, D), F32, kind="ExternalOutput").ap()
    block_kernel(nc, t)
    r = run_bass_kernel_spmd(nc, [feed], core_ids=[0])
    return r.results[0]["out_dram"]
```
